# Optimizing a Trainium2 kernel written in Bass

```python
import numpy as np
import jax
import jax.numpy as jnp

def _softmax(x, axis=-1):
    return jax.nn.softmax(x, axis=axis)

def _gelu(x):
    return jax.nn.gelu(x, approximate=True)

def _silu(x):
    return jax.nn.silu(x)

def _sigmoid(x):
    return jax.nn.sigmoid(x)

def _layernorm(x, axis=-1, eps=1e-05):
    m = jnp.mean(x, axis=axis, keepdims=True)
    v = jnp.var(x, axis=axis, keepdims=True)
    return (x - m) / jnp.sqrt(v + eps)

def _scatter_add(tgt, idx, src, axis=0):
    return tgt.at[idx].add(src)

def _segment_sum(src, seg, n):
    return jax.ops.segment_sum(src, seg, n)
kernel_name = 'mk_rec_standalone_d1_rec_r8_7264b7'

def setup_inputs(seed: int=0):
    np.random.seed(seed)
    _w = jnp.asarray

    def _rec_inputs():
        import jax
        import jax.numpy as jnp
        _rk = jax.random.key(seed)
        r_numerical_features = 8.7408e-05 + 1.0001 * jax.random.normal(jax.random.fold_in(_rk, 1), (2048, 13), jnp.float32)
        r_cat_features = jnp.stack([jax.random.randint(jax.random.fold_in(jax.random.fold_in(_rk, 2), 0), (2048,), 4, 99994, jnp.int32), jax.random.randint(jax.random.fold_in(jax.random.fold_in(_rk, 2), 1), (2048,), 0, 99999, jnp.int32), jax.random.randint(jax.random.fold_in(jax.random.fold_in(_rk, 2), 2), (2048,), 1, 99998, jnp.int32), jax.random.randint(jax.random.fold_in(jax.random.fold_in(_rk, 2), 3), (2048,), 2, 99995, jnp.int32), jax.random.randint(jax.random.fold_in(jax.random.fold_in(_rk, 2), 4), (2048,), 0, 99999, jnp.int32), jax.random.randint(jax.random.fold_in(jax.random.fold_in(_rk, 2), 5), (2048,), 4, 12500, jnp.int32), jax.random.randint(jax.random.fold_in(jax.random.fold_in(_rk, 2), 6), (2048,), 0, 99999, jnp.int32), jax.random.randint(jax.random.fold_in(jax.random.fold_in(_rk, 2), 7), (2048,), 0, 99993, jnp.int32), jax.random.randint(jax.random.fold_in(jax.random.fold_in(_rk, 2), 8), (2048,), 2, 99998, jnp.int32), jax.random.randint(jax.random.fold_in(jax.random.fold_in(_rk, 2), 9), (2048,), 2, 12500, jnp.int32), jax.random.randint(jax.random.fold_in(jax.random.fold_in(_rk, 2), 10), (2048,), 2, 12500, jnp.int32), jax.random.randint(jax.random.fold_in(jax.random.fold_in(_rk, 2), 11), (2048,), 2, 99998, jnp.int32), jax.random.randint(jax.random.fold_in(jax.random.fold_in(_rk, 2), 12), (2048,), 1, 99995, jnp.int32), jax.random.randint(jax.random.fold_in(jax.random.fold_in(_rk, 2), 13), (2048,), 5, 12500, jnp.int32), jax.random.randint(jax.random.fold_in(jax.random.fold_in(_rk, 2), 14), (2048,), 8, 12500, jnp.int32), jax.random.randint(jax.random.fold_in(jax.random.fold_in(_rk, 2), 15), (2048,), 0, 99999, jnp.int32), jax.random.randint(jax.random.fold_in(jax.random.fold_in(_rk, 2), 16), (2048,), 9, 99999, jnp.int32), jax.random.randint(jax.random.fold_in(jax.random.fold_in(_rk, 2), 17), (2048,), 2, 99998, jnp.int32), jax.random.randint(jax.random.fold_in(jax.random.fold_in(_rk, 2), 18), (2048,), 3, 12500, jnp.int32), jax.random.randint(jax.random.fold_in(jax.random.fold_in(_rk, 2), 19), (2048,), 6, 99997, jnp.int32), jax.random.randint(jax.random.fold_in(jax.random.fold_in(_rk, 2), 20), (2048,), 5, 12500, jnp.int32), jax.random.randint(jax.random.fold_in(jax.random.fold_in(_rk, 2), 21), (2048,), 0, 99999, jnp.int32), jax.random.randint(jax.random.fold_in(jax.random.fold_in(_rk, 2), 22), (2048,), 1, 12500, jnp.int32), jax.random.randint(jax.random.fold_in(jax.random.fold_in(_rk, 2), 23), (2048,), 4, 99999, jnp.int32), jax.random.randint(jax.random.fold_in(jax.random.fold_in(_rk, 2), 24), (2048,), 0, 99997, jnp.int32), jax.random.randint(jax.random.fold_in(jax.random.fold_in(_rk, 2), 25), (2048,), 3, 12500, jnp.int32)], axis=0)
        return (r_numerical_features, r_cat_features)
    r_numerical_features, r_cat_features = _rec_inputs()

    def _L0_rec_setup():
        import jax, jax.numpy as jnp
        import numpy as np
        NUM_TABLES = 26
        VOCAB = 12500
        EMB_DIM = 64
        BATCH = 4096
        NUM_NUMERICAL = 13
        DEEP_UNITS = [1024, 1024, 512, 256, 1]
        key = jax.random.key(seed)
        ks = jax.random.split(key, 16)
        inp = {}
        inp['numerical_features'] = jax.random.normal(ks[0], (BATCH, NUM_NUMERICAL), dtype=jnp.float32)
        inp['cat_features'] = jax.random.randint(ks[1], (NUM_TABLES, BATCH), 0, VOCAB, dtype=jnp.int32)
        inp['emb_tables'] = jax.random.normal(ks[2], (NUM_TABLES, VOCAB, EMB_DIM), dtype=jnp.float32) * 0.05
        in_dim = NUM_NUMERICAL + NUM_TABLES * EMB_DIM
        inp['w_wide'] = jax.random.normal(ks[3], (in_dim, 1), dtype=jnp.float32) * (1.0 / np.sqrt(in_dim))
        inp['b_wide'] = jnp.zeros((1,), dtype=jnp.float32)
        dims = [in_dim] + DEEP_UNITS
        for i in range(len(DEEP_UNITS)):
            inp[f'w{i}'] = jax.random.normal(ks[4 + i], (dims[i], dims[i + 1]), dtype=jnp.float32) * (1.0 / np.sqrt(dims[i]))
            inp[f'b{i}'] = jnp.zeros((dims[i + 1],), dtype=jnp.float32)
        return inp
    _L0_rec_all = _L0_rec_setup()
    _L0_rec_in = {k: v for k, v in _L0_rec_all.items() if k in ('emb_tables', 'w_wide', 'b_wide', 'w0', 'b0', 'w1', 'b1', 'w2', 'b2', 'w3', 'b3', 'w4', 'b4')}
    del _L0_rec_all
    return {'r_numerical_features': r_numerical_features, 'r_cat_features': r_cat_features, 'L0_rec_emb_tables': _L0_rec_in['emb_tables'], 'L0_rec_w_wide': _L0_rec_in['w_wide'], 'L0_rec_b_wide': _L0_rec_in['b_wide'], 'L0_rec_w0': _L0_rec_in['w0'], 'L0_rec_b0': _L0_rec_in['b0'], 'L0_rec_w1': _L0_rec_in['w1'], 'L0_rec_b1': _L0_rec_in['b1'], 'L0_rec_w2': _L0_rec_in['w2'], 'L0_rec_b2': _L0_rec_in['b2'], 'L0_rec_w3': _L0_rec_in['w3'], 'L0_rec_b3': _L0_rec_in['b3'], 'L0_rec_w4': _L0_rec_in['w4'], 'L0_rec_b4': _L0_rec_in['b4']}

def reference(r_numerical_features, r_cat_features, L0_rec_emb_tables, L0_rec_w_wide, L0_rec_b_wide, L0_rec_w0, L0_rec_b0, L0_rec_w1, L0_rec_b1, L0_rec_w2, L0_rec_b2, L0_rec_w3, L0_rec_b3, L0_rec_w4, L0_rec_b4):
    import jax
    import jax.numpy as jnp

    def _L0_rec_ref(numerical_features, cat_features, emb_tables, w_wide, b_wide, w0, b0, w1, b1, w2, b2, w3, b3, w4, b4):
        import jax, jax.numpy as jnp
        import numpy as np
        NUM_TABLES = 26
        VOCAB = 12500
        EMB_DIM = 64
        BATCH = 4096
        NUM_NUMERICAL = 13
        DEEP_UNITS = [1024, 1024, 512, 256, 1]
        table_ids = jnp.arange(NUM_TABLES)[:, None]
        emb = emb_tables[table_ids, cat_features]
        emb_flat = jnp.transpose(emb, (1, 0, 2)).reshape(emb.shape[1], NUM_TABLES * EMB_DIM)
        x = jnp.concatenate([numerical_features, emb_flat], axis=1)
        linear_out = jax.nn.relu(x @ w_wide + b_wide)
        h = x
        for w, b in ((w0, b0), (w1, b1), (w2, b2), (w3, b3)):
            h = jax.nn.relu(h @ w + b)
        dnn_out = h @ w4 + b4
        return jax.nn.sigmoid(dnn_out + linear_out)
    y = _L0_rec_ref(r_numerical_features, r_cat_features, L0_rec_emb_tables, L0_rec_w_wide, L0_rec_b_wide, L0_rec_w0, L0_rec_b0, L0_rec_w1, L0_rec_b1, L0_rec_w2, L0_rec_b2, L0_rec_w3, L0_rec_b3, L0_rec_w4, L0_rec_b4)
    return y

_drawn_inputs = setup_inputs


def setup_inputs(seed=0):
    import zlib

    import numpy as np

    out = dict(_drawn_inputs(seed))
    spreads = {'L0_rec_b0': (0.0, 0.8),
     'L0_rec_b1': (0.0, 0.571),
     'L0_rec_b2': (0.0, 0.321),
     'L0_rec_b3': (0.0, 2.0)}
    factors = {'L0_rec_emb_tables': 4.665,
     'L0_rec_w0': 5.392,
     'L0_rec_w1': 5.933,
     'L0_rec_w3': 6.642,
     'L0_rec_w_wide': 4.164}
    for name, (base, spread) in spreads.items():
        noise = np.random.default_rng([zlib.crc32(name.encode()), seed]).standard_normal(out[name].shape)
        drawn = base * np.exp(spread * noise) if base else spread * noise
        out[name] = jnp.asarray(drawn.astype(out[name].dtype))
    for name, factor in factors.items():
        out[name] = (out[name] * factor).astype(out[name].dtype)
    return out
```

```python
import concourse.bass as bass
import concourse.mybir as mybir
from contextlib import ExitStack

F32 = mybir.dt.float32
F32R = mybir.dt.float32r
I32 = mybir.dt.int32
ALU = mybir.AluOpType
ACT = mybir.ActivationFunctionType

P = 128
BATCH = 2048
TABLES, VOCAB, EMB = 26, 12500, 64
NUM = 13
UNITS = [512, 512, 512, 512]
UNIT = max(UNITS)
BLK = 32
G = P // BLK
QF = TABLES // G
Q = QF + 1
KT0 = TABLES * EMB // P
D0, D1, D2, D3 = 1024, 1024, 512, 256
M0, M1, M2, M3 = D0 // P, D1 // P, D2 // P, D3 // P
WS = 4
XS = 2
HS = 4
ST1, ST2 = KT0, KT0 + M0
STREAM = ST2 + M1 // 2
SPLIT = M0 + M1 + M2
TILES = SPLIT + M3
ADDS = KT0 + 1
SUBS = BATCH // P
C0, C6 = BATCH // BLK, BATCH // (2 * BLK)
NB = M0 + M1 + M2 + M3
COL_W4, COL_WW, COL_WN, COL_BW, COL_B4 = NB, NB + M3, NB + M3 + KT0, NB + M3 + KT0 + 1, NB + M3 + KT0 + 2
COL_AT = COL_B4 + 1
COLS = COL_AT + 2


def uses(s):
    return len(range(s, STREAM, WS))


def build(nc, num_t, cat, emb, w0e, w0n, w1, w2, w3, params, out):
    ctx = ExitStack()
    with ctx:
        def sb(name, shape, dt=F32):
            return ctx.enter_context(nc.sbuf_tensor(name, shape, dt))

        def sem(name):
            return ctx.enter_context(nc.semaphore(name))

        par = sb("par", [P, COLS])
        ones = sb("ones", [P, 1])
        cat_in = sb("cat_in", [P, QF * C0 + C6], I32)
        idx = sb("idx", [P, QF * C0 + C6], I32)
        idx_now = sb("idx_now", [P, QF * UNIT // BLK + UNIT // (2 * BLK)], I32)
        rows = [sb(f"rows{q}", [P, UNIT // BLK if q < QF else UNIT // (2 * BLK), EMB]) for q in range(Q)]
        turned = sb("turned", [P, 2, UNIT])
        cat_f, wrap = turned[:, 0, 0:QF * C0 + C6], turned[:, 1, 0:QF * C0 + C6]
        last_x = sb("last_x", [P, UNIT])
        x_h = sb("x_h", [P, XS, 2, UNIT], F32R)
        x_l = sb("x_l", [P, XS, 2, UNIT], F32R)
        num_in = sb("num_in", [NUM, UNIT])
        num_x = sb("num_x", [P, UNIT], F32R)
        num_w = sb("num_w", [P, D0], F32R)
        wide = sb("wide", [P, UNIT])
        wide_all = sb("wide_all", [P, UNIT])
        w_in = sb("w_in", [P, WS, D0])
        w_h = sb("w_h", [P, WS, D0], F32R)
        w_l = sb("w_l", [P, WS, D0], F32R)
        w3_h = sb("w3_h", [P, M2, D3], F32R)
        w3_l = sb("w3_l", [P, M2, D3], F32R)
        h_f = sb("h_f", [P, HS, UNIT])
        even_h = sb("even_h", [P, M0, UNIT], F32R)
        even_l = sb("even_l", [P, M0, UNIT], F32R)
        odd_h = sb("odd_h", [P, M1, UNIT], F32R)
        odd_l = sb("odd_l", [P, M1, UNIT], F32R)
        relu_w = sb("relu_w", [P, UNIT // P])
        logit = sb("logit", [P, UNIT // P])
        prob = sb("prob", [P, SUBS])
        bank = [ctx.enter_context(nc.psum_tensor(f"bank{m}", [P, 512], F32)) for m in range(8)]
        LAST = bank[6]

        params_here, cat_here = sem("params_here"), sem("cat_here")
        w3_here, wn_here = sem("w3_here"), sem("wn_here")
        num_here = sem("num_here")
        w_here = [sem(f"w_here{s}") for s in range(WS)]
        rows_here = [sem(f"rows_here{q}") for q in range(Q)]
        const_set, idx_step, idx_ready, idx_copied = sem("const_set"), sem("idx_step"), sem("idx_ready"), sem("idx_copied")
        fixed_hi, fixed_lo = sem("fixed_hi"), sem("fixed_lo")
        rows_free, rows_turned, last_placed = sem("rows_free"), sem("rows_turned"), sem("last_placed")
        x_hi, x_split = sem("x_hi"), sem("x_split")
        num_hi, num_split = sem("num_hi"), sem("num_split")
        wide_added, wide_copied = sem("wide_added"), sem("wide_copied")
        w_hi, w_split, w_used = sem("w_hi"), sem("w_split"), sem("w_used")
        summed, relu_done, h_hi, h_split = sem("summed"), sem("relu_done"), sem("h_hi"), sem("h_split")
        logits_done, wide_relu, logits_read, probs_done = sem("logits_done"), sem("wide_relu"), sem("logits_read"), sem("probs_done")
        stored = sem("stored")

        block = ctx.enter_context(nc.Block())

        def wait(eng, s, value):
            if not (isinstance(value, int) and value <= 0):
                eng.wait_ge(s, value)

        ends = {ST1 - 1: M0, ST2 - 1: M0 + M1, STREAM - 1: SPLIT}
        USED = STREAM - len(ends)

        def wait_used(eng, u, kt):
            if kt in ends:
                eng.wait_ge(summed, TILES * u + ends[kt])
            else:
                eng.wait_ge(w_used, USED * u + kt + 1 - sum(e < kt for e in ends))

        def raw(ap):
            return ap.bitcast(F32)

        wn_in = h_f[0:NUM, 0:2, :].rearrange("p s n -> p (s n)")
        w3_in = h_f[:, 2:4, :].rearrange("p s n -> p (s n)").rearrange("p (k n) -> p k n", k=M2)

        @block.sync
        def _(sp):
            sp.dma_start(cat_in[:], cat).then_inc(cat_here, 16)
            sp.dma_start(par[:], params).then_inc(params_here, 16)
            sp.dma_start(wn_in, w0n).then_inc(wn_here, 16)
            sp.dma_start(num_in[:], num_t[:, 0:UNIT]).then_inc(num_here, 16)
            sp.dma_start(w3_in, w3.rearrange("(k p) n -> p k n", p=P)).then_inc(w3_here, 16)

            def stream(u, more):
                for kt in range(STREAM):
                    if kt < WS:
                        wait(sp, w_split, STREAM * u)
                    else:
                        sp.wait_ge(w_split, STREAM * u + kt + 1 - WS)
                    to = w_in[:, kt % WS, :]
                    if kt < ST1:
                        src = w0e[kt]
                    elif kt < ST2:
                        src = w1[(kt - ST1) * P:(kt - ST1 + 1) * P, :]
                    else:
                        to = to.rearrange("p (k n) -> p k n", k=2)
                        src = w2.rearrange("(j k p) n -> j p k n", k=2, p=P)[kt - ST2]
                    sp.dma_start(to, src).then_inc(w_here[kt % WS], 16)
                    if more and kt == ST1:
                        sp.wait_ge(num_split, u + 1)
                        sp.dma_start(num_in[:], num_t[:, bass.ts(u + 1, UNIT)]).then_inc(num_here, 16)

            with sp.Fori(0, len(UNITS) - 1) as u:
                stream(u, True)
            stream(len(UNITS) - 1, False)
            sp.wait_ge(probs_done, len(UNITS))
            sp.dma_start(out, prob[:]).then_inc(stored, 16)
            sp.wait_ge(stored, 16)

        @block.gpsimd
        def _(pool):
            pool.memset(ones[:], 1.0).then_inc(const_set, 1)
            pool.memset(raw(num_w[:]), 0.0)
            pool.memset(raw(num_x[:]), 0.0).then_inc(const_set, 1)

            def gather(u, index, index_last):
                for q in range(Q):
                    if not isinstance(u, int):
                        pool.wait_ge(rows_turned, Q * u + q + 1 - Q)
                        pool.sem_inc(rows_free, 1)
                    for c in range(UNIT // BLK if q < QF else UNIT // (2 * BLK)):
                        at = index(q, c) if q < QF else index_last(c)
                        pool.indirect_dma_start(
                            rows[q][:, c, :], None, emb, bass.IndirectOffsetOnAxis(ap=at, axis=0)).then_inc(rows_here[q], 16)

            pool.wait_ge(idx_ready, 1)
            gather(0, lambda q, c: idx[:, q * C0 + c:q * C0 + c + 1],
                   lambda c: idx[:, QF * C0 + c:QF * C0 + c + 1])
            n, n6 = UNIT // BLK, UNIT // (2 * BLK)
            with pool.Fori(1, len(UNITS)) as u:
                for q in range(Q):
                    pool.wait_ge(rows_here[q], 16 * (n if q < QF else n6) * u)
                pool.tensor_copy(idx_now[:, 0:QF * n].rearrange("p (q c) -> p q c", q=QF),
                                 idx[:, 0:QF * C0].rearrange("p (q c) -> p q c", q=QF)[:, :, bass.ts(u, n)])
                pool.tensor_copy(idx_now[:, QF * n:QF * n + n6],
                                 idx[:, QF * C0:QF * C0 + C6][:, bass.ts(u, n6)]).then_inc(idx_copied, 1)
                pool.wait_ge(idx_copied, u)
                gather(u, lambda q, c: idx_now[:, q * n + c:q * n + c + 1],
                       lambda c: idx_now[:, QF * n + c:QF * n + c + 1])

        @block.scalar
        def _(act):
            def split_w(u, kt):
                s = kt % WS
                act.wait_ge(w_here[s], 16 * (uses(s) * u + kt // WS + 1))
                if kt >= WS:
                    wait_used(act, u, kt - WS)
                elif not (isinstance(u, int) and u == 0):
                    wait_used(act, u - 1, STREAM - 1 - (STREAM - 1 - kt) % WS)
                nc.scalar.copy(w_h[:, s, :], w_in[:, s, :]).then_inc(w_hi, 1)

            def split_x(u, q):
                act.wait_ge(rows_turned, Q * u + q + 1)
                if q == QF:
                    t6 = turned[:, 0, :].rearrange("p (b c i) -> p b c i", b=2, i=BLK)
                    x6 = last_x[:].rearrange("p (c h i) -> p c h i", h=2, i=BLK)
                    for h in range(2):
                        for b in range(2):
                            last = nc.scalar.copy(x6[64 * b:64 * b + 64, :, h, :], t6[64 * h:64 * h + 64, b, :, :])
                    last.then_inc(last_placed, 1)
                    act.wait_ge(last_placed, u + 1)
                if q >= XS:
                    wait_used(act, u, 2 * (q - XS) + 1)
                elif not (isinstance(u, int) and u == 0):
                    wait_used(act, u - 1, ST1 - 1)
                if q == QF:
                    nc.scalar.copy(x_h[:, q % XS, 0, :], last_x[:]).then_inc(x_hi, 1)
                else:
                    nc.scalar.copy(x_h[:, q % XS, :, :], turned[:]).then_inc(x_hi, 1)

            def split_num(u):
                act.wait_ge(num_here, 16 * (u + 1))
                nc.scalar.copy(num_x[0:NUM, :], num_in[:])
                nc.scalar.copy(num_x[64:64 + NUM, :], num_in[:]).then_inc(num_hi, 1)

            def evacuate(u, layer):
                t0 = (0, M0, M0 + M1, SPLIT)[layer]
                count = (M0, M1, M2, M3)[layer]
                dst = (even_h, odd_h, even_h, None)[layer]

                def relu(m):
                    t = t0 + m
                    act.wait_ge(summed, TILES * u + t + 1)
                    if layer == 3:
                        act.wait_ge(h_split, SPLIT * u + SPLIT)
                    elif t >= HS:
                        act.wait_ge(h_split, SPLIT * u + t + 1 - HS)
                    elif t < M3:
                        wait(act, logits_done, u)
                    nc.scalar.activation(h_f[:, m % HS, :], bank[m if layer < 3 else 4 + m][:], ACT.Relu,
                                         bias=par[:, t:t + 1]).then_inc(relu_done, 1)

                def hi(m):
                    act.wait_ge(relu_done, TILES * u + t0 + m + 1)
                    nc.scalar.copy(dst[:, m, :], h_f[:, m % HS, :]).then_inc(h_hi, 1)

                for m in range(count):
                    relu(m)
                    if m and layer < 3:
                        hi(m - 1)
                if layer < 3:
                    hi(count - 1)

            def start_unit(u):
                for q in range(XS):
                    split_x(u, q)
                split_num(u)

            def start_stream(u):
                for kt in range(WS):
                    split_w(u, kt)

            def unit(u, more):
                for q in range(XS, Q):
                    split_w(u, 2 * q)
                    split_w(u, 2 * q + 1)
                    split_x(u, q)
                for kt in (2 * Q, 2 * Q + 1):
                    split_w(u, kt)
                act.wait_ge(wide_added, ADDS * (u + 1))
                wait(act, logits_done, u)
                nc.scalar.copy(wide_all[:], wide[:]).then_inc(wide_copied, 1)
                evacuate(u, 0)
                for kt in range(2 * Q + 2, ST2 + 1):
                    split_w(u, kt)
                evacuate(u, 1)
                for kt in range(ST2 + 1, STREAM):
                    split_w(u, kt)
                if more:
                    start_unit(u + 1)
                evacuate(u, 2)
                if more:
                    start_stream(u + 1)
                evacuate(u, 3)
                act.wait_ge(logits_read, u + 1)
                nc.scalar.activation(prob[:, bass.ts(u, UNIT // P)], logit[:], ACT.Sigmoid,
                                     bias=par[:, COL_B4:COL_B4 + 1]).then_inc(probs_done, 1)

            act.wait_ge(w3_here, 16)
            nc.scalar.copy(w3_h[:], w3_in).then_inc(fixed_hi, 1)
            act.wait_ge(wn_here, 16)
            act.wait_ge(const_set, 2)
            nc.scalar.copy(num_w[0:NUM, :], wn_in)
            nc.scalar.copy(num_w[BLK:BLK + NUM, :], wn_in).then_inc(fixed_hi, 1)
            act.wait_ge(params_here, 16)
            start_stream(0)
            start_unit(0)
            with act.Fori(0, len(UNITS) - 1) as u:
                unit(u, True)
            unit(len(UNITS) - 1, False)

        @block.vector
        def _(dve):
            def row_numbers():
                dve.wait_ge(cat_here, 16)
                nc.vector.tensor_copy(cat_f, cat_in[:]).then_inc(idx_step, 1)
                dve.wait_ge(idx_step, 1)
                nc.vector.tensor_scalar(wrap, cat_f, 0.0, float(VOCAB), ALU.is_lt, ALU.mult).then_inc(idx_step, 1)
                dve.wait_ge(idx_step, 2)
                nc.vector.tensor_tensor(cat_f, cat_f, wrap, ALU.add).then_inc(idx_step, 1)
                dve.wait_ge(idx_step, 3)
                nc.vector.tensor_scalar(wrap, cat_f, float(VOCAB - 1), 0.0, ALU.min, ALU.max).then_inc(idx_step, 1)
                dve.wait_ge(idx_step, 4)
                dve.wait_ge(params_here, 16)
                for q in range(QF):
                    nc.vector.tensor_scalar(idx[:, q * C0:(q + 1) * C0], wrap[:, q * C0:(q + 1) * C0],
                                            par[:, COL_AT:COL_AT + 1], float(q * G * VOCAB), ALU.add, ALU.add)
                nc.vector.tensor_scalar(idx[:, QF * C0:], wrap[:, QF * C0:],
                                        par[:, COL_AT + 1:COL_AT + 2], None, ALU.add).then_inc(idx_ready, 1)

            def split_w(u, kt):
                s = kt % WS
                dve.wait_ge(w_hi, STREAM * u + kt + 1)
                nc.vector.tensor_tensor(w_l[:, s, :], w_in[:, s, :], raw(w_h[:, s, :]), ALU.subtract).then_inc(w_split, 1)

            def add_wide(u, n, x, kt):
                weight = par[:, COL_WW + kt:COL_WW + kt + 1]
                if n == 0:
                    wait(dve, wide_copied, u)
                    nc.vector.tensor_scalar(wide[:], x, weight, None, ALU.mult).then_inc(wide_added, 1)
                else:
                    dve.wait_ge(wide_added, ADDS * u + n)
                    nc.vector.scalar_tensor_tensor(wide[:], x, weight, wide[:], ALU.mult, ALU.add).then_inc(wide_added, 1)

            def split_x(u, q):
                n = UNIT // BLK if q < QF else UNIT // (2 * BLK)
                dve.wait_ge(rows_here[q], 16 * n * (u + 1))
                wait(dve, x_split, Q * u + q)
                if q < QF:
                    to = turned[:].rearrange("p b (c i) -> p c b i", i=BLK)
                else:
                    to = turned[:, 0, :].rearrange("p (b c i) -> p c b i", b=2, i=BLK)
                nc.vector.transpose(to, rows[q][:].rearrange("p c (b i) -> p c b i", i=BLK)).then_inc(rows_turned, 1)
                if q < QF:
                    dve.wait_ge(rows_turned, Q * u + q + 1)
                    for b in range(2):
                        add_wide(u, 2 * q + b + (q >= XS), turned[:, b, :], 2 * q + b)
                    dve.wait_ge(x_hi, Q * u + q + 1)
                    nc.vector.tensor_tensor(x_l[:, q % XS, :, :], turned[:], raw(x_h[:, q % XS, :, :]),
                                            ALU.subtract).then_inc(x_split, 1)
                else:
                    dve.wait_ge(last_placed, u + 1)
                    add_wide(u, ADDS - 1, last_x[:], KT0 - 1)
                    dve.wait_ge(x_hi, Q * u + q + 1)
                    nc.vector.tensor_tensor(x_l[:, q % XS, 0, :], last_x[:], raw(x_h[:, q % XS, 0, :]),
                                            ALU.subtract).then_inc(x_split, 1)

            def split_num(u):
                dve.wait_ge(num_hi, u + 1)
                dve.wait_ge(wide_added, ADDS * u + 2 * XS)
                nc.vector.scalar_tensor_tensor(wide[0:NUM, :], num_in[:], par[0:NUM, COL_WN:COL_WN + 1], wide[0:NUM, :],
                                               ALU.mult, ALU.add).then_inc(wide_added, 1)
                for g in (1, 3):
                    last = nc.vector.tensor_tensor(num_x[BLK * g:BLK * g + NUM, :], num_in[:], raw(num_x[0:NUM, :]), ALU.subtract)
                last.then_inc(num_split, 1)

            def evacuate(u, layer):
                t0 = (0, M0, M0 + M1)[layer]
                hi, lo = ((even_h, even_l), (odd_h, odd_l), (even_h, even_l))[layer]
                for m in range((M0, M1, M2)[layer]):
                    dve.wait_ge(h_hi, SPLIT * u + t0 + m + 1)
                    nc.vector.tensor_tensor(lo[:, m, :], h_f[:, m % HS, :], raw(hi[:, m, :]), ALU.subtract).then_inc(h_split, 1)

            def start_unit(u):
                for q in range(XS):
                    split_x(u, q)
                split_num(u)

            def start_stream(u):
                for kt in range(WS):
                    split_w(u, kt)

            def unit(u, more):
                for q in range(XS, Q):
                    split_w(u, 2 * q)
                    split_w(u, 2 * q + 1)
                    split_x(u, q)
                for kt in (2 * Q, 2 * Q + 1):
                    split_w(u, kt)
                evacuate(u, 0)
                for kt in range(2 * Q + 2, ST2 + 1):
                    split_w(u, kt)
                evacuate(u, 1)
                for kt in range(ST2 + 1, STREAM):
                    split_w(u, kt)
                if more:
                    start_unit(u + 1)
                evacuate(u, 2)
                if more:
                    start_stream(u + 1)
                dve.wait_ge(logits_done, u + 1)
                nc.vector.tensor_scalar(relu_w[:], LAST[:, 8:8 + UNIT // P], par[:, COL_BW:COL_BW + 1], 0.0,
                                        ALU.add, ALU.max).then_inc(wide_relu, 1)
                dve.wait_ge(wide_relu, u + 1)
                nc.vector.tensor_tensor(logit[:], LAST[:, 0:UNIT // P], relu_w[:], ALU.add).then_inc(logits_read, 1)

            row_numbers()
            dve.wait_ge(fixed_hi, 1)
            nc.vector.tensor_tensor(w3_l[:], w3_in, raw(w3_h[:]), ALU.subtract).then_inc(fixed_lo, 1)
            dve.wait_ge(fixed_hi, 2)
            for g in (2, 3):
                last = nc.vector.tensor_tensor(num_w[BLK * g:BLK * g + NUM, :], wn_in, raw(num_w[0:NUM, :]), ALU.subtract)
            last.then_inc(fixed_lo, 1)
            dve.wait_ge(params_here, 16)
            start_stream(0)
            start_unit(0)
            with dve.Fori(0, len(UNITS) - 1) as u:
                unit(u, True)
            unit(len(UNITS) - 1, False)

        @block.tensor
        def _(pe):
            def products(dst, wh, wl, m, xh, xl, start, stop):
                cols = slice(m * P, (m + 1) * P)
                nc.tensor.matmul(dst, wh[:, cols], xh, start=start, stop=False)
                nc.tensor.matmul(dst, wh[:, cols], xl, start=False, stop=False)
                return nc.tensor.matmul(dst, wl[:, cols], xh, start=False, stop=stop)

            def input_tile(u, kt, s, xs, b, stop=False):
                pe.wait_ge(w_split, STREAM * u + kt + 1)
                for m in range(M0):
                    last = products(bank[m][:], w_h[:, s, :], w_l[:, s, :], m, x_h[:, xs, b, :], x_l[:, xs, b, :], False, stop)
                    if stop:
                        last.then_inc(summed, 1)
                if not stop:
                    last.then_inc(w_used, 1)

            def unit(u):
                pe.wait_ge(num_split, u + 1)
                wait(pe, relu_done, TILES * u)
                for m in range(M0):
                    if m == 6:
                        wait(pe, logits_read, u)
                    nc.tensor.matmul(bank[m][:], num_w[:, m * P:(m + 1) * P], num_x[:], start=True, stop=False)
                with pe.Fori(0, QF // 2) as j:
                    for i in range(2):
                        pe.wait_ge(x_split, Q * u + 2 * j + i + 1)
                        for b in range(2):
                            input_tile(u, 4 * j + 2 * i + b, 2 * i + b, i, b)
                pe.wait_ge(x_split, Q * (u + 1))
                input_tile(u, KT0 - 1, (KT0 - 1) % WS, QF % XS, 0, stop=True)
                for k in range(M0):
                    s = (KT0 + k) % WS
                    pe.wait_ge(w_split, STREAM * u + KT0 + k + 1)
                    pe.wait_ge(h_split, SPLIT * u + k + 1)
                    for m in range(M1):
                        if k == 0:
                            pe.wait_ge(relu_done, TILES * u + m + 1)
                        last = products(bank[m][:], w_h[:, s, :], w_l[:, s, :], m, even_h[:, k, :], even_l[:, k, :],
                                        k == 0, k == M0 - 1)
                        if k == M0 - 1:
                            last.then_inc(summed, 1)
                    if k < M0 - 1:
                        last.then_inc(w_used, 1)
                for k in range(M1):
                    s, half = (ST2 + k // 2) % WS, slice(k % 2 * D2, (k % 2 + 1) * D2)
                    pe.wait_ge(w_split, STREAM * u + ST2 + k // 2 + 1)
                    pe.wait_ge(h_split, SPLIT * u + M0 + k + 1)
                    for m in range(M2):
                        if k == 0:
                            pe.wait_ge(relu_done, TILES * u + M0 + m + 1)
                        last = products(bank[m][:], w_h[:, s, half], w_l[:, s, half], m, odd_h[:, k, :], odd_l[:, k, :],
                                        k == 0, k == M1 - 1)
                        if k == M1 - 1:
                            last.then_inc(summed, 1)
                    if k % 2 and k < M1 - 1:
                        last.then_inc(w_used, 1)
                for k in range(M2):
                    pe.wait_ge(h_split, SPLIT * u + M0 + M1 + k + 1)
                    for m in range(M3):
                        if k == 0:
                            pe.wait_ge(relu_done, TILES * u + M0 + 4 + m + 1)
                        last = products(bank[4 + m][:], w3_h[:, k, :], w3_l[:, k, :], m, even_h[:, k, :], even_l[:, k, :],
                                        k == 0, k == M2 - 1)
                        if k == M2 - 1:
                            last.then_inc(summed, 1)
                pe.wait_ge(wide_copied, u + 1)
                for c in range(UNIT // P):
                    nc.tensor.matmul(LAST[:, 8 + c:9 + c], wide_all[:, c * P:(c + 1) * P], ones[:], start=True, stop=True)
                pe.wait_ge(relu_done, TILES * u + TILES)
                for c in range(UNIT // P):
                    for k in range(M3):
                        last = nc.tensor.matmul(LAST[:, c:c + 1], h_f[:, k, c * P:(c + 1) * P], par[:, COL_W4 + k:COL_W4 + k + 1],
                                                start=k == 0, stop=k == M3 - 1)
                last.then_inc(logits_done, 1)

            pe.wait_ge(fixed_lo, 2)
            pe.wait_ge(params_here, 16)
            pe.wait_ge(const_set, 2)
            with pe.Fori(0, len(UNITS)) as u:
                unit(u)


def kernel(r_numerical_features, r_cat_features, L0_rec_emb_tables, L0_rec_w_wide, L0_rec_b_wide, L0_rec_w0, L0_rec_b0,
           L0_rec_w1, L0_rec_b1, L0_rec_w2, L0_rec_b2, L0_rec_w3, L0_rec_b3, L0_rec_w4, L0_rec_b4):
    import numpy as np
    import concourse.bacc as bacc
    from concourse.bass_utils import run_bass_kernel_spmd

    def tiles(w):
        w = w[NUM:].reshape(TABLES, 2, BLK, -1)
        full = w[:QF * G].reshape(QF, G, 2, BLK, -1).transpose(0, 2, 1, 3, 4).reshape(2 * QF, P, -1)
        last = w[QF * G:].transpose(1, 0, 2, 3).reshape(1, P, -1)
        return np.concatenate([full, last])

    def columns(v):
        return np.asarray(v).reshape(-1, P).T

    w_wide, w0 = np.asarray(L0_rec_w_wide), np.asarray(L0_rec_w0)
    table = np.arange(P).reshape(P, 1) // BLK
    first_row = np.concatenate([table, QF * G + table % 2], axis=1) * VOCAB
    w_wide_num = np.concatenate([w_wide[:NUM], np.zeros((P - NUM, 1), w_wide.dtype)])
    params = np.concatenate([
        columns(L0_rec_b0), columns(L0_rec_b1), columns(L0_rec_b2), columns(L0_rec_b3), columns(L0_rec_w4),
        tiles(w_wide)[:, :, 0].T, w_wide_num,
        np.broadcast_to(np.asarray(L0_rec_b_wide), (P, 1)), np.broadcast_to(np.asarray(L0_rec_b4), (P, 1)),
        first_row.astype(np.float32)], axis=1)
    cat = np.asarray(r_cat_features)
    cat_full = cat[:QF * G].reshape(QF, G, C0, BLK).transpose(1, 3, 0, 2).reshape(P, QF * C0)
    cat_last = cat[QF * G:].reshape(2, C6, 2, BLK).transpose(2, 0, 3, 1).reshape(P, C6)
    arrays = {
        "num_t": np.asarray(r_numerical_features).T, "cat": np.concatenate([cat_full, cat_last], axis=1),
        "emb": np.asarray(L0_rec_emb_tables).reshape(TABLES * VOCAB, EMB),
        "w0e": tiles(w0), "w0n": w0[:NUM], "w1": np.asarray(L0_rec_w1), "w2": np.asarray(L0_rec_w2),
        "w3": np.asarray(L0_rec_w3), "params": params,
    }
    arrays = {n: np.ascontiguousarray(a) for n, a in arrays.items()}
    nc = bacc.Bacc("TRN2", target_bir_lowering=False, num_devices=1)
    aps = [nc.dram_tensor(n, a.shape, mybir.dt.from_np(a.dtype), kind="ExternalInput").ap() for n, a in arrays.items()]
    out = nc.dram_tensor("probs", (P, SUBS), F32, kind="ExternalOutput").ap()
    build(nc, *aps, out)
    r = run_bass_kernel_spmd(nc, [arrays], core_ids=[0])
    return r.results[0]["probs"].T.reshape(BATCH, 1)
```

```python
import concourse.bass as bass
import concourse.mybir as mybir
from contextlib import ExitStack

F32 = mybir.dt.float32
F32R = mybir.dt.float32r
I32 = mybir.dt.int32
ALU = mybir.AluOpType
ACT = mybir.ActivationFunctionType

P = 128
BATCH = 2048
TABLES, VOCAB, EMB = 26, 12500, 64
NUM = 13
UNITS = [256, 256, 512, 512, 512]
UNIT = max(UNITS)
SHORT = 2
BLK = 32
G = P // BLK
QF = TABLES // G
Q = QF + 1
KT0 = TABLES * EMB // P
D0, D1, D2, D3 = 1024, 1024, 512, 256
M0, M1, M2, M3 = D0 // P, D1 // P, D2 // P, D3 // P
WS = 4
XS = 2
HS = 4
ST1, ST2 = KT0, KT0 + M0
STREAM = ST2 + M1 // 2
FIRST = (0, M0, M0 + M1, M0 + M1 + M2)
TILES = FIRST[3] + M3
ADDS = KT0 + 1
C0, C6 = BATCH // BLK, BATCH // (2 * BLK)
NB = M0 + M1 + M2 + M3
COL_W4, COL_WW, COL_WN, COL_BW, COL_B4 = NB, NB + M3, NB + M3 + KT0, NB + M3 + KT0 + 1, NB + M3 + KT0 + 2
COL_AT = COL_B4 + 1
COLS = COL_AT + 2 * Q


def before(u, size):
    if isinstance(u, int):
        return sum(UNITS[:u]) // size
    return u * (UNIT // size) - (UNIT * SHORT - sum(UNITS[:SHORT])) // size


def after(u, n, size):
    return before(u, size) + n // size


def each_unit(eng, body):
    for u in range(SHORT):
        body(u, UNITS[u], UNITS[u + 1])
    with eng.Fori(SHORT, len(UNITS) - 1) as u:
        body(u, UNIT, UNIT)
    body(len(UNITS) - 1, UNITS[-1], 0)


def slot(kt):
    return kt % WS if kt < STREAM - 1 else 1


def in_slot(kt):
    same = [k for k in range(STREAM) if slot(k) == slot(kt)]
    return same.index(kt) + 1, len(same)


def before_in_slot(kt):
    same = [k for k in range(STREAM) if slot(k) == slot(kt)]
    return same[same.index(kt) - 1], kt == same[0]


def build(nc, num_t, cat, emb, w0e, w0n, w1, w2, w3, params, out):
    ctx = ExitStack()
    with ctx:
        def sb(name, shape, dt=F32):
            return ctx.enter_context(nc.sbuf_tensor(name, shape, dt))

        def sem(name):
            return ctx.enter_context(nc.semaphore(name))

        par = sb("par", [P, COLS])
        ones = sb("ones", [P, 1], F32R)
        w4_h = sb("w4_h", [P, M3], F32R)
        w4_l = sb("w4_l", [P, M3], F32R)
        cat_in = sb("cat_in", [P, QF * C0 + C6], I32)
        idx = sb("idx", [P, QF * C0 + C6], I32)
        idx_now = sb("idx_now", [P, QF * UNIT // BLK + UNIT // (2 * BLK)], I32)
        rows = [sb(f"rows{q}", [P, UNIT // BLK if q < QF else UNIT // (2 * BLK), EMB]) for q in range(Q)]
        turned = sb("turned", [P, 2, UNIT])
        cat_f, wrap = turned[:, 0, 0:QF * C0 + C6], turned[:, 1, 0:QF * C0 + C6]
        last_x = sb("last_x", [P, UNIT])
        x_h = sb("x_h", [P, XS, 2, UNIT], F32R)
        x_l = sb("x_l", [P, XS, 2, UNIT], F32R)
        num_in = sb("num_in", [BLK + NUM, UNIT])
        num_x = sb("num_x", [P, UNIT], F32R)
        num_w = sb("num_w", [P, D0], F32R)
        wide = sb("wide", [P, UNIT])
        wide_h = sb("wide_h", [P, UNIT], F32R)
        wide_l = sb("wide_l", [P, UNIT], F32R)
        w_in = sb("w_in", [P, WS, D0])
        w_h = sb("w_h", [P, WS, D0], F32R)
        w_l = sb("w_l", [P, WS, D0], F32R)
        w3_h = sb("w3_h", [P, M2, D3], F32R)
        w3_l = sb("w3_l", [P, M2, D3], F32R)
        h_f = sb("h_f", [P, HS, UNIT])
        even_h = sb("even_h", [P, M0, UNIT], F32R)
        even_l = sb("even_l", [P, M0, UNIT], F32R)
        odd_h = sb("odd_h", [P, M1, UNIT], F32R)
        odd_l = sb("odd_l", [P, M1, UNIT], F32R)
        relu_w = sb("relu_w", [1, UNIT])
        logit = sb("logit", [1, UNIT])
        prob = sb("prob", [1, UNIT])
        bank = [ctx.enter_context(nc.psum_tensor(f"bank{m}", [P, 512], F32)) for m in range(8)]
        LINEAR, LOGIT = bank[6], bank[5]
        banks = (range(8), range(8), range(4), (4, 5))

        params_here, cat_here = sem("params_here"), sem("cat_here")
        w3_here, wn_here = sem("w3_here"), sem("wn_here")
        num_here = sem("num_here")
        w_here = [sem(f"w_here{s}") for s in range(WS)]
        rows_here = [sem(f"rows_here{q}") for q in range(Q)]
        const_set, idx_step, idx_ready, idx_copied = sem("const_set"), sem("idx_step"), sem("idx_ready"), sem("idx_copied")
        fixed_hi, fixed_lo = sem("fixed_hi"), sem("fixed_lo")
        rows_free, rows_turned, last_placed = sem("rows_free"), sem("rows_turned"), sem("last_placed")
        x_hi, x_split = sem("x_hi"), sem("x_split")
        num_hi, num_split = sem("num_hi"), sem("num_split")
        wide_added, wide_hi, wide_split = sem("wide_added"), sem("wide_hi"), sem("wide_split")
        w_hi, w_split, w_used = sem("w_hi"), sem("w_split"), sem("w_used")
        summed, h_hi, h_split = sem("summed"), sem("h_hi"), sem("h_split")
        relu_done = [sem("relu_even"), sem("relu_odd")]
        linear_done, wide_relu = sem("linear_done"), sem("wide_relu")
        logits_done, logits_read, probs_done = sem("logits_done"), sem("logits_read"), sem("probs_done")
        stored = sem("stored")

        block = ctx.enter_context(nc.Block())

        def wait(eng, s, value):
            if not (isinstance(value, int) and value <= 0):
                eng.wait_ge(s, value)

        ends = {ST1 - 1: FIRST[1], ST2 - 1: FIRST[2], STREAM - 1: FIRST[3]}
        USED = STREAM - len(ends)

        def wait_used(eng, u, kt):
            if kt in ends:
                eng.wait_ge(summed, TILES * u + ends[kt])
            else:
                eng.wait_ge(w_used, USED * u + kt + 1 - sum(e < kt for e in ends))

        def wait_relu(eng, u, t):
            eng.wait_ge(relu_done[t % 2], TILES // 2 * u + t // 2 + 1)

        def wait_slot(eng, u, t, m):
            if m < HS:
                wait(eng, h_split, TILES * u + t - m)
            else:
                eng.wait_ge(h_split, TILES * u + t + 1 - HS)

        def raw(ap):
            return ap.bitcast(F32)

        wn_in = h_f[0:2 * BLK + NUM, 0:2, :].rearrange("p s n -> p (s n)")
        w3_in = h_f[:, 2:4, :].rearrange("p s n -> p (s n)").rearrange("p (k n) -> p k n", k=M2)

        @block.sync
        def _(sp):
            sp.dma_start(cat_in[:], cat).then_inc(cat_here, 16)
            sp.dma_start(par[:], params).then_inc(params_here, 16)
            sp.dma_start(wn_in, w0n).then_inc(wn_here, 16)
            sp.dma_start(num_in[:, 0:UNITS[0]], num_t[:, 0:UNITS[0]]).then_inc(num_here, 16)
            sp.dma_start(w3_in, w3.rearrange("(k p) n -> p k n", p=P)).then_inc(w3_here, 16)

            def stream(u, n, n_next):
                for kt in range(STREAM):
                    earlier, last_unit = before_in_slot(kt)
                    if not (last_unit and isinstance(u, int) and u == 0):
                        sp.wait_ge(w_split, STREAM * (u - last_unit) + earlier + 1)
                    to = w_in[:, slot(kt), :]
                    if kt < ST1:
                        src = w0e[kt]
                    elif kt < ST2:
                        src = w1[(kt - ST1) * P:(kt - ST1 + 1) * P, :]
                    else:
                        to = to.rearrange("p (k n) -> p k n", k=2)
                        src = w2.rearrange("(j k p) n -> j p k n", k=2, p=P)[kt - ST2]
                    sp.dma_start(to, src).then_inc(w_here[slot(kt)], 16)
                    if n_next and kt == ST1:
                        sp.wait_ge(num_split, u + 1)
                        sp.dma_start(num_in[:, 0:n_next], num_t[:, bass.ds(after(u, n, 1), n_next)]).then_inc(num_here, 16)

            each_unit(sp, stream)

        @block.gpsimd
        def _(pool):
            pool.memset(raw(ones[:]), 1.0).then_inc(const_set, 1)
            pool.memset(raw(num_w[:]), 0.0)
            pool.memset(raw(num_x[:]), 0.0).then_inc(const_set, 1)

            def gather(u, n, index, index_last):
                for q in range(Q):
                    if isinstance(u, int) and u == 0:
                        pool.wait_ge(idx_ready, min(q, 1) + 1)
                    else:
                        pool.wait_ge(rows_turned, Q * u + q + 1 - Q)
                        pool.sem_inc(rows_free, 1)
                    for c in range(n // BLK if q < QF else n // (2 * BLK)):
                        at = index(q, c) if q < QF else index_last(c)
                        pool.indirect_dma_start(
                            rows[q][:, c, :], None, emb, bass.IndirectOffsetOnAxis(ap=at, axis=0)).then_inc(rows_here[q], 16)

            def unit(u, n, n_next):
                b, b6 = before(u, BLK), before(u, 2 * BLK)
                if isinstance(u, int):
                    gather(u, n, lambda q, c: idx[:, q * C0 + b + c:q * C0 + b + c + 1],
                           lambda c: idx[:, QF * C0 + b6 + c:QF * C0 + b6 + c + 1])
                    return
                nb, nb6 = n // BLK, n // (2 * BLK)
                for q in range(Q):
                    pool.wait_ge(rows_here[q], 16 * (b if q < QF else b6))
                pool.tensor_copy(idx_now[:, 0:QF * nb].rearrange("p (q c) -> p q c", q=QF),
                                 idx[:, 0:QF * C0].rearrange("p (q c) -> p q c", q=QF)[:, :, bass.ds(b, nb)])
                pool.tensor_copy(idx_now[:, QF * nb:QF * nb + nb6],
                                 idx[:, QF * C0:QF * C0 + C6][:, bass.ds(b6, nb6)]).then_inc(idx_copied, 1)
                pool.wait_ge(idx_copied, u + 1 - SHORT)
                gather(u, n, lambda q, c: idx_now[:, q * nb + c:q * nb + c + 1],
                       lambda c: idx_now[:, QF * nb + c:QF * nb + c + 1])

            each_unit(pool, unit)

        @block.scalar
        def _(act):
            def split_w(u, kt):
                s = slot(kt)
                so_far, per_unit = in_slot(kt)
                act.wait_ge(w_here[s], 16 * (per_unit * u + so_far))
                earlier, last_unit = before_in_slot(kt)
                if not (last_unit and isinstance(u, int) and u == 0):
                    wait_used(act, u - last_unit, earlier)
                nc.scalar.copy(w_h[:, s, :], w_in[:, s, :]).then_inc(w_hi, 1)

            def split_x(u, n, q):
                act.wait_ge(rows_turned, Q * u + q + 1)
                if q == QF:
                    t6 = turned[:, 0, 0:n].rearrange("p (b c i) -> p b c i", b=2, i=BLK)
                    x6 = last_x[:, 0:n].rearrange("p (c h i) -> p c h i", h=2, i=BLK)
                    for h in range(2):
                        for b in range(2):
                            last = nc.scalar.copy(x6[64 * b:64 * b + 64, :, h, :], t6[64 * h:64 * h + 64, b, :, :])
                    last.then_inc(last_placed, 1)
                    act.wait_ge(last_placed, u + 1)
                if q >= XS:
                    wait_used(act, u, 2 * (q - XS) + 1)
                elif not (isinstance(u, int) and u == 0):
                    wait_used(act, u - 1, ST1 - 1)
                if q == QF:
                    nc.scalar.copy(x_h[:, q % XS, 0, 0:n], last_x[:, 0:n]).then_inc(x_hi, 1)
                else:
                    nc.scalar.copy(x_h[:, q % XS, :, 0:n], turned[:, :, 0:n]).then_inc(x_hi, 1)

            def split_num(u, n):
                act.wait_ge(num_here, 16 * (u + 1))
                nc.scalar.copy(num_x[0:BLK + NUM, 0:n], num_in[:, 0:n]).then_inc(num_hi, 1)

            def evacuate(u, n, layer):
                dst, t0 = (even_h, odd_h, even_h, odd_h)[layer], FIRST[layer]
                count = len(banks[layer])

                def relu(m):
                    act.wait_ge(summed, TILES * u + t0 + m + 1)
                    wait_slot(act, u, t0 + m, m)
                    nc.scalar.activation(h_f[:, m % HS, 0:n], bank[banks[layer][m]][:, 0:n], ACT.Relu,
                                         bias=par[:, t0 + m:t0 + m + 1]).then_inc(relu_done[0], 1)

                def hi(m):
                    wait_relu(act, u, t0 + m)
                    nc.scalar.copy(dst[:, m, 0:n], h_f[:, m % HS, 0:n]).then_inc(h_hi, 1)

                relu(0)
                for m in range(0, count, 2):
                    hi(m)
                    if m + 2 < count:
                        relu(m + 2)
                    hi(m + 1)

            def start_unit(u, n):
                split_x(u, n, 0)
                split_num(u, n)

            def unit(u, n, n_next):
                for q in range(XS, Q):
                    split_w(u, 2 * q)
                    split_w(u, 2 * q + 1)
                    split_x(u, n, q)
                split_w(u, 2 * Q)
                evacuate(u, n, 0)
                split_w(u, 2 * Q + 1)
                act.wait_ge(wide_added, ADDS * (u + 1))
                wait(act, linear_done, u)
                nc.scalar.copy(wide_h[:, 0:n], wide[:, 0:n]).then_inc(wide_hi, 1)
                for kt in range(2 * Q + 2, ST2 - 1):
                    split_w(u, kt)
                if n_next:
                    start_unit(u + 1, n_next)
                for kt in range(ST2 - 1, STREAM - 2):
                    split_w(u, kt)
                evacuate(u, n, 1)
                for kt in range(STREAM - 2, STREAM):
                    split_w(u, kt)
                if n_next:
                    split_w(u + 1, 0)
                    split_x(u + 1, n_next, 1)
                evacuate(u, n, 2)
                act.wait_ge(linear_done, u + 1)
                wait(act, logits_read, u)
                nc.scalar.activation(relu_w[:, 0:n], LINEAR[0:1, 0:n], ACT.Relu,
                                     bias=par[0:1, COL_BW:COL_BW + 1]).then_inc(wide_relu, 1)
                evacuate(u, n, 3)
                if n_next:
                    for kt in range(1, WS):
                        split_w(u + 1, kt)
                act.wait_ge(logits_read, u + 1)
                wait(act, stored, 16 * u)
                nc.scalar.activation(prob[:, 0:n], logit[:, 0:n], ACT.Sigmoid, bias=par[0:1, COL_B4:COL_B4 + 1]).then_inc(probs_done, 1)
                act.wait_ge(probs_done, u + 1)
                act.dma_start(out[:, bass.ds(before(u, P) * P, n)], prob[:, 0:n]).then_inc(stored, 16)

            act.wait_ge(w3_here, 16)
            nc.scalar.copy(w3_h[:], w3_in).then_inc(fixed_hi, 1)
            act.wait_ge(wn_here, 16)
            act.wait_ge(const_set, 2)
            nc.scalar.copy(num_w[0:2 * BLK + NUM, :], wn_in).then_inc(fixed_hi, 1)
            act.wait_ge(params_here, 16)
            nc.scalar.copy(w4_h[:], par[:, COL_W4:COL_W4 + M3]).then_inc(fixed_hi, 1)
            for kt in range(WS):
                split_w(0, kt)
            start_unit(0, UNITS[0])
            split_x(0, UNITS[0], 1)
            each_unit(act, unit)
            act.wait_ge(stored, 16 * len(UNITS))

        @block.vector
        def _(dve):
            def row_numbers(part, cols, groups):
                nc.vector.tensor_scalar(wrap[:, cols], cat_in[:, cols], 0.0, float(VOCAB), ALU.is_lt, ALU.mult).then_inc(idx_step, 1)
                dve.wait_ge(idx_step, 2 * part + 1)
                for q in groups:
                    of = slice(q * C0, (q + 1) * C0) if q < QF else slice(QF * C0, QF * C0 + C6)
                    last = nc.vector.scalar_tensor_tensor(cat_f[:, of], cat_in[:, of], par[:, COL_AT + q:COL_AT + q + 1], wrap[:, of],
                                                          ALU.add, ALU.add)
                last.then_inc(idx_step, 1)
                dve.wait_ge(idx_step, 2 * part + 2)
                for q in groups:
                    of = slice(q * C0, (q + 1) * C0) if q < QF else slice(QF * C0, QF * C0 + C6)
                    last = nc.vector.tensor_scalar(idx[:, of], cat_f[:, of], par[:, COL_AT + q:COL_AT + q + 1],
                                                   par[:, COL_AT + Q + q:COL_AT + Q + q + 1], ALU.max, ALU.min)
                last.then_inc(idx_ready, 1)

            def split_w(u, kt):
                s = slot(kt)
                dve.wait_ge(w_hi, STREAM * u + kt + 1)
                nc.vector.tensor_tensor(w_l[:, s, :], w_in[:, s, :], raw(w_h[:, s, :]), ALU.subtract).then_inc(w_split, 1)

            def add_wide(u, n, term, x, kt):
                weight = par[:, COL_WW + kt:COL_WW + kt + 1]
                if term == 0:
                    wait(dve, wide_split, u)
                    nc.vector.tensor_scalar(wide[:, 0:n], x, weight, None, ALU.mult).then_inc(wide_added, 1)
                else:
                    dve.wait_ge(wide_added, ADDS * u + term)
                    nc.vector.scalar_tensor_tensor(wide[:, 0:n], x, weight, wide[:, 0:n], ALU.mult, ALU.add).then_inc(wide_added, 1)

            def split_x(u, n, q):
                size = BLK if q < QF else 2 * BLK
                dve.wait_ge(rows_here[q], 16 * after(u, n, size))
                wait(dve, x_split, Q * u + q)
                if q > 0:
                    dve.wait_ge(wide_added, ADDS * u + 2 * q + 1)
                else:
                    wait(dve, wide_added, ADDS * u)
                if q < QF:
                    to = turned[:, :, 0:n].rearrange("p b (c i) -> p c b i", i=BLK)
                else:
                    to = turned[:, 0, 0:n].rearrange("p (b c i) -> p c b i", b=2, i=BLK)
                nc.vector.transpose(to, rows[q][:, 0:n // size, :].rearrange("p c (b i) -> p c b i", i=BLK)).then_inc(rows_turned, 1)
                if q < QF:
                    dve.wait_ge(rows_turned, Q * u + q + 1)
                    add_wide(u, n, 2 * q + (q > 0), turned[:, 0, 0:n], 2 * q)
                    dve.wait_ge(x_hi, Q * u + q + 1)
                    nc.vector.tensor_tensor(x_l[:, q % XS, :, 0:n], turned[:, :, 0:n], raw(x_h[:, q % XS, :, 0:n]),
                                            ALU.subtract).then_inc(x_split, 1)
                    add_wide(u, n, 2 * q + 1 + (q > 0), turned[:, 1, 0:n], 2 * q + 1)
                else:
                    dve.wait_ge(last_placed, u + 1)
                    add_wide(u, n, ADDS - 1, last_x[:, 0:n], KT0 - 1)
                    dve.wait_ge(x_hi, Q * u + q + 1)
                    nc.vector.tensor_tensor(x_l[:, q % XS, 0, 0:n], last_x[:, 0:n], raw(x_h[:, q % XS, 0, 0:n]),
                                            ALU.subtract).then_inc(x_split, 1)

            def split_num(u, n):
                dve.wait_ge(num_hi, u + 1)
                dve.wait_ge(wide_added, ADDS * u + 2)
                nc.vector.scalar_tensor_tensor(wide[0:NUM, 0:n], num_in[0:NUM, 0:n], par[0:NUM, COL_WN:COL_WN + 1], wide[0:NUM, 0:n],
                                               ALU.mult, ALU.add).then_inc(wide_added, 1)
                nc.vector.tensor_tensor(num_x[2 * BLK:2 * BLK + NUM, 0:n], num_in[0:NUM, 0:n], raw(num_x[0:NUM, 0:n]),
                                        ALU.subtract).then_inc(num_split, 1)

            def evacuate(u, n, layer):
                hi, lo = ((even_h, even_l), (odd_h, odd_l))[layer % 2]
                t0 = FIRST[layer]

                def relu(m):
                    dve.wait_ge(summed, TILES * u + t0 + m + 1)
                    wait_slot(dve, u, t0 + m, m)
                    nc.vector.tensor_scalar(h_f[:, m % HS, 0:n], bank[banks[layer][m]][:, 0:n], par[:, t0 + m:t0 + m + 1], 0.0,
                                            ALU.add, ALU.max).then_inc(relu_done[1], 1)

                def split(m):
                    dve.wait_ge(h_hi, TILES * u + t0 + m + 1)
                    nc.vector.tensor_tensor(lo[:, m, 0:n], h_f[:, m % HS, 0:n], raw(hi[:, m, 0:n]), ALU.subtract).then_inc(h_split, 1)

                for m in range(0, len(banks[layer]), 2):
                    relu(m + 1)
                    split(m)
                    split(m + 1)

            def start_unit(u, n):
                split_x(u, n, 0)
                split_num(u, n)

            def unit(u, n, n_next):
                for q in range(XS, Q):
                    split_w(u, 2 * q)
                    split_w(u, 2 * q + 1)
                    split_x(u, n, q)
                split_w(u, 2 * Q)
                evacuate(u, n, 0)
                split_w(u, 2 * Q + 1)
                dve.wait_ge(wide_hi, u + 1)
                nc.vector.tensor_tensor(wide_l[:, 0:n], wide[:, 0:n], raw(wide_h[:, 0:n]), ALU.subtract).then_inc(wide_split, 1)
                for kt in range(2 * Q + 2, ST2 - 1):
                    split_w(u, kt)
                if n_next:
                    start_unit(u + 1, n_next)
                for kt in range(ST2 - 1, STREAM - 2):
                    split_w(u, kt)
                evacuate(u, n, 1)
                for kt in range(STREAM - 2, STREAM):
                    split_w(u, kt)
                if n_next:
                    split_w(u + 1, 0)
                    split_x(u + 1, n_next, 1)
                evacuate(u, n, 2)
                evacuate(u, n, 3)
                if n_next:
                    split_w(u + 1, 1)
                dve.wait_ge(wide_relu, u + 1)
                dve.wait_ge(logits_done, u + 1)
                nc.vector.tensor_tensor(logit[:, 0:n], LOGIT[0:1, 0:n], relu_w[:, 0:n], ALU.add).then_inc(logits_read, 1)
                if n_next:
                    for kt in range(2, WS):
                        split_w(u + 1, kt)

            dve.wait_ge(cat_here, 16)
            dve.wait_ge(params_here, 16)
            row_numbers(0, slice(0, C0), (0,))
            row_numbers(1, slice(C0, QF * C0 + C6), range(1, Q))
            dve.wait_ge(idx_ready, 2)
            dve.wait_ge(fixed_hi, 1)
            nc.vector.tensor_tensor(w3_l[:], w3_in, raw(w3_h[:]), ALU.subtract).then_inc(fixed_lo, 1)
            dve.wait_ge(fixed_hi, 2)
            nc.vector.tensor_tensor(num_w[BLK:BLK + NUM, :], wn_in[0:NUM, :], raw(num_w[0:NUM, :]), ALU.subtract).then_inc(fixed_lo, 1)
            dve.wait_ge(fixed_hi, 3)
            nc.vector.tensor_tensor(w4_l[:], par[:, COL_W4:COL_W4 + M3], raw(w4_h[:]), ALU.subtract).then_inc(fixed_lo, 1)
            for kt in range(WS):
                split_w(0, kt)
            start_unit(0, UNITS[0])
            split_x(0, UNITS[0], 1)
            each_unit(dve, unit)

        @block.tensor
        def _(pe):
            def products(dst, wh, wl, m, xh, xl, stop):
                cols = m if isinstance(m, slice) else slice(m * P, (m + 1) * P)
                nc.tensor.matmul(dst, wh[:, cols], xh, start=False, stop=False)
                nc.tensor.matmul(dst, wh[:, cols], xl, start=False, stop=False)
                return nc.tensor.matmul(dst, wl[:, cols], xh, start=False, stop=stop)

            def first_tile(u, t, sums, freed, wh, wl, xh, xl):
                pe.wait_ge(h_hi, TILES * u + t + 1)
                for m, dst in enumerate(sums):
                    cols = slice(m * P, (m + 1) * P)
                    wait_relu(pe, u, freed + m)
                    nc.tensor.matmul(dst, wh[:, cols], xh, start=True, stop=False)
                    nc.tensor.matmul(dst, wl[:, cols], xh, start=False, stop=False)
                    if m == 1:
                        pe.wait_ge(h_split, TILES * u + t + 1)
                        nc.tensor.matmul(sums[0], wh[:, 0:P], xl, start=False, stop=False)
                    if m >= 1:
                        last = nc.tensor.matmul(dst, wh[:, cols], xl, start=False, stop=False)
                return last

            def input_tile(u, n, s, xs, b, tiles=range(M0), stop=False):
                for m in tiles:
                    last = products(bank[m][:, 0:n], w_h[:, s, :], w_l[:, s, :], m, x_h[:, xs, b, 0:n], x_l[:, xs, b, 0:n], stop)
                    if stop:
                        last.then_inc(summed, 1)
                return last

            def numerical(u, n, m):
                nc.tensor.matmul(bank[m][:, 0:n], num_w[:, m * P:(m + 1) * P], num_x[:, 0:n], start=True, stop=False)

            early, fifth, late = (0, 1, 2, 3, 7), (4,), (5, 6)

            def begin(u, n):
                pe.wait_ge(num_split, u + 1)
                if not (isinstance(u, int) and u == 0):
                    for t in (FIRST[3] - 2, FIRST[3] - 1):
                        wait_relu(pe, u - 1, t)
                for m in early:
                    numerical(u, n, m)
                pe.wait_ge(x_split, Q * u + 1)
                pe.wait_ge(w_split, STREAM * u + 1)
                input_tile(u, n, 0, 0, 0, early)

            def unit(u, n, n_next):
                for m in fifth:
                    numerical(u, n, m)
                input_tile(u, n, 0, 0, 0, fifth)
                pe.wait_ge(w_split, STREAM * u + 2)
                input_tile(u, n, 1, 0, 1, early + fifth)
                wait(pe, logits_read, u)
                for m in late:
                    numerical(u, n, m)
                input_tile(u, n, 0, 0, 0, late).then_inc(w_used, 1)
                input_tile(u, n, 1, 0, 1, late).then_inc(w_used, 1)
                with pe.Fori(0, 2) as j:
                    for i in range(2):
                        pe.wait_ge(x_split, Q * u + 2 * j + i + 2)
                        for b in range(2):
                            pe.wait_ge(w_split, STREAM * u + 4 * j + 2 * i + b + 3)
                            input_tile(u, n, (2 * i + b + 2) % WS, (i + 1) % XS, b).then_inc(w_used, 1)
                pe.wait_ge(x_split, Q * u + QF)
                for b in range(2):
                    pe.wait_ge(w_split, STREAM * u + KT0 - 2 + b)
                    input_tile(u, n, (KT0 - 3 + b) % WS, (QF - 1) % XS, b).then_inc(w_used, 1)
                pe.wait_ge(x_split, Q * (u + 1))
                pe.wait_ge(w_split, STREAM * u + KT0)
                input_tile(u, n, (KT0 - 1) % WS, QF % XS, 0, stop=True)
                s = slot(KT0)
                pe.wait_ge(w_split, STREAM * u + KT0 + 1)
                first_tile(u, FIRST[0], [bank[m][:, 0:n] for m in banks[1]], FIRST[0], w_h[:, s, :], w_l[:, s, :],
                           even_h[:, 0, 0:n], even_l[:, 0, 0:n]).then_inc(w_used, 1)
                for k in range(1, M0):
                    s = slot(KT0 + k)
                    pe.wait_ge(w_split, STREAM * u + KT0 + k + 1)
                    pe.wait_ge(h_split, TILES * u + FIRST[0] + k + 1)
                    for m in range(M1):
                        last = products(bank[m][:, 0:n], w_h[:, s, :], w_l[:, s, :], m, even_h[:, k, 0:n], even_l[:, k, 0:n],
                                        k == M0 - 1)
                        if k == M0 - 1:
                            last.then_inc(summed, 1)
                    if k < M0 - 1:
                        last.then_inc(w_used, 1)
                s = slot(ST2)
                pe.wait_ge(w_split, STREAM * u + ST2 + 1)
                first_tile(u, FIRST[1], [bank[m][:, 0:n] for m in banks[2]], FIRST[1], w_h[:, s, :], w_l[:, s, :],
                           odd_h[:, 0, 0:n], odd_l[:, 0, 0:n])
                for k in range(1, M1):
                    s, half = slot(ST2 + k // 2), slice(k % 2 * D2, (k % 2 + 1) * D2)
                    pe.wait_ge(w_split, STREAM * u + ST2 + k // 2 + 1)
                    pe.wait_ge(h_split, TILES * u + FIRST[1] + k + 1)
                    for m in range(M2):
                        last = products(bank[m][:, 0:n], w_h[:, s, half], w_l[:, s, half], m, odd_h[:, k, 0:n], odd_l[:, k, 0:n],
                                        k == M1 - 1)
                        if k == M1 - 1:
                            last.then_inc(summed, 1)
                    if k % 2 and k < M1 - 1:
                        last.then_inc(w_used, 1)
                pe.wait_ge(wide_split, u + 1)
                wait_relu(pe, u, FIRST[1] + 6)
                nc.tensor.matmul(LINEAR[0:1, 0:n], ones[:], wide_h[:, 0:n], start=True, stop=False)
                nc.tensor.matmul(LINEAR[0:1, 0:n], ones[:], wide_l[:, 0:n], start=False, stop=True).then_inc(linear_done, 1)
                first_tile(u, FIRST[2], [bank[m][:, 0:n] for m in banks[3]], FIRST[1] + banks[3][0], w3_h[:, 0, :], w3_l[:, 0, :],
                           even_h[:, 0, 0:n], even_l[:, 0, 0:n])
                for k in range(1, M2):
                    pe.wait_ge(h_split, TILES * u + FIRST[2] + k + 1)
                    for m in range(M3):
                        last = products(bank[banks[3][m]][:, 0:n], w3_h[:, k, :], w3_l[:, k, :], m, even_h[:, k, 0:n], even_l[:, k, 0:n],
                                        k == M2 - 1)
                        if k == M2 - 1:
                            last.then_inc(summed, 1)
                if n_next:
                    begin(u + 1, n_next)
                wait_relu(pe, u, TILES - 1)
                pe.wait_ge(h_hi, TILES * u + FIRST[3] + 1)
                nc.tensor.matmul(LOGIT[0:1, 0:n], w4_h[:, 0:1], odd_h[:, 0, 0:n], start=True, stop=False)
                nc.tensor.matmul(LOGIT[0:1, 0:n], w4_l[:, 0:1], odd_h[:, 0, 0:n], start=False, stop=False)
                pe.wait_ge(h_split, TILES * u + FIRST[3] + 1)
                nc.tensor.matmul(LOGIT[0:1, 0:n], w4_h[:, 0:1], odd_l[:, 0, 0:n], start=False, stop=False)
                for k in range(1, M3):
                    pe.wait_ge(h_split, TILES * u + FIRST[3] + k + 1)
                    last = products(LOGIT[0:1, 0:n], w4_h, w4_l, slice(k, k + 1), odd_h[:, k, 0:n], odd_l[:, k, 0:n],
                                    k == M3 - 1)
                last.then_inc(logits_done, 1)

            pe.wait_ge(fixed_lo, 3)
            pe.wait_ge(const_set, 2)
            pe.wait_ge(x_split, 2)
            begin(0, UNITS[0])
            each_unit(pe, unit)


def kernel(r_numerical_features, r_cat_features, L0_rec_emb_tables, L0_rec_w_wide, L0_rec_b_wide, L0_rec_w0, L0_rec_b0,
           L0_rec_w1, L0_rec_b1, L0_rec_w2, L0_rec_b2, L0_rec_w3, L0_rec_b3, L0_rec_w4, L0_rec_b4):
    import numpy as np
    import concourse.bacc as bacc
    from concourse.bass_utils import run_bass_kernel_spmd

    def tiles(w):
        w = w[NUM:].reshape(TABLES, 2, BLK, -1)
        full = w[:QF * G].reshape(QF, G, 2, BLK, -1).transpose(0, 2, 1, 3, 4).reshape(2 * QF, P, -1)
        last = w[QF * G:].transpose(1, 0, 2, 3).reshape(1, P, -1)
        return np.concatenate([full, last])

    def stacked(a, times):
        out = np.zeros((BLK * (times - 1) + NUM, a.shape[1]), a.dtype)
        for g in range(times):
            out[BLK * g:BLK * g + NUM] = a
        return out

    def columns(v):
        return np.asarray(v).reshape(-1, P).T

    w_wide, w0 = np.asarray(L0_rec_w_wide), np.asarray(L0_rec_w0)
    table = np.arange(P).reshape(P, 1) // BLK
    first_row = np.concatenate([G * q + table if q < QF else G * q + table % 2 for q in range(Q)], axis=1) * VOCAB
    w_wide_num = np.concatenate([w_wide[:NUM], np.zeros((P - NUM, 1), w_wide.dtype)])
    params = np.concatenate([
        columns(L0_rec_b0), columns(L0_rec_b1), columns(L0_rec_b2), columns(L0_rec_b3), columns(L0_rec_w4),
        tiles(w_wide)[:, :, 0].T, w_wide_num,
        np.broadcast_to(np.asarray(L0_rec_b_wide), (P, 1)), np.broadcast_to(np.asarray(L0_rec_b4), (P, 1)),
        first_row.astype(np.float32), (first_row + VOCAB - 1).astype(np.float32)], axis=1)
    cat = np.asarray(r_cat_features)
    cat_full = cat[:QF * G].reshape(QF, G, C0, BLK).transpose(1, 3, 0, 2).reshape(P, QF * C0)
    cat_last = cat[QF * G:].reshape(2, C6, 2, BLK).transpose(2, 0, 3, 1).reshape(P, C6)
    arrays = {
        "num_t": stacked(np.asarray(r_numerical_features).T, 2), "cat": np.concatenate([cat_full, cat_last], axis=1),
        "emb": np.asarray(L0_rec_emb_tables).reshape(TABLES * VOCAB, EMB),
        "w0e": tiles(w0), "w0n": stacked(w0[:NUM], 3), "w1": np.asarray(L0_rec_w1), "w2": np.asarray(L0_rec_w2),
        "w3": np.asarray(L0_rec_w3), "params": params,
    }
    arrays = {n: np.ascontiguousarray(a) for n, a in arrays.items()}
    nc = bacc.Bacc("TRN2", target_bir_lowering=False, num_devices=1)
    aps = [nc.dram_tensor(n, a.shape, mybir.dt.from_np(a.dtype), kind="ExternalInput").ap() for n, a in arrays.items()]
    out = nc.dram_tensor("probs", (1, BATCH), F32, kind="ExternalOutput").ap()
    build(nc, *aps, out)
    r = run_bass_kernel_spmd(nc, [arrays], core_ids=[0])
    return r.results[0]["probs"].reshape(BATCH, 1)
```
